# Optimizing a Trainium2 kernel written in Bass

```python
import numpy as np
import jax
import jax.numpy as jnp

def _softmax(x, axis=-1):
    return jax.nn.softmax(x, axis=axis)

def _gelu(x):
    return jax.nn.gelu(x, approximate=True)

def _silu(x):
    return jax.nn.silu(x)

def _sigmoid(x):
    return jax.nn.sigmoid(x)

def _layernorm(x, axis=-1, eps=1e-05):
    m = jnp.mean(x, axis=axis, keepdims=True)
    v = jnp.var(x, axis=axis, keepdims=True)
    return (x - m) / jnp.sqrt(v + eps)

def _scatter_add(tgt, idx, src, axis=0):
    return tgt.at[idx].add(src)

def _segment_sum(src, seg, n):
    return jax.ops.segment_sum(src, seg, n)
kernel_name = 'mk_adaln_ffn_d2_seqx_r4_24f8ba'

def setup_inputs(seed: int=0):
    np.random.seed(seed)
    _w = jnp.asarray

    def _rec_inputs():
        import jax
        import jax.numpy as jnp
        _rk = jax.random.key(seed)
        x = -7.109e-05 + 0.9999 * jax.random.normal(jax.random.fold_in(_rk, 1), (64, 64, 1024), jnp.float32)
        _lenS = 64 - jax.random.randint(jax.random.fold_in(_rk, 7), (64,), 0, max(1, 64 // 4) + 1, jnp.int32)
        _lenS2 = 64 - jax.random.randint(jax.random.fold_in(_rk, 8), (64,), 0, max(1, 64 // 4) + 1, jnp.int32)
        itok_B_0_15 = jax.random.randint(jax.random.fold_in(_rk, 11), (64,), 0, 16, jnp.int32)
        itok_B_3_7 = jax.random.randint(jax.random.fold_in(_rk, 12), (64,), 3, 8, jnp.int32)
        return (x, itok_B_0_15, itok_B_3_7)
    x, itok_B_0_15, itok_B_3_7 = _rec_inputs()

    def _L0_cond_setup():
        import jax, jax.numpy as jnp
        import numpy as np
        NUM_CONDITIONS = 16
        IN_CH = 64
        OUT_CH = 64
        B = 64
        T = 1024
        key = jax.random.key(seed)
        k_x, k_w, k_c = jax.random.split(key, 3)
        x = jax.random.normal(k_x, (B, IN_CH, T), dtype=jnp.float32)
        bound = float(np.sqrt(6.0 / IN_CH))
        weights = jax.random.uniform(k_w, (NUM_CONDITIONS, IN_CH, OUT_CH), dtype=jnp.float32, minval=-bound, maxval=bound)
        condition = jax.random.randint(k_c, (B,), 0, NUM_CONDITIONS, dtype=jnp.int64)
        return {'x': x, 'weights': weights, 'condition': condition}
    _L0_cond_all = _L0_cond_setup()
    _L0_cond_in = {k: v for k, v in _L0_cond_all.items() if k in ('weights',)}
    del _L0_cond_all

    def _L0_ffn_setup():
        import jax, jax.numpy as jnp
        import numpy as np
        BATCH, TOK, DIM, OUT = (4, 512, 1024, 1024)
        E, R, TOP_K = (8, 16, 2)
        SCALING = 16.0 / R
        key = jax.random.key(seed)
        ks = jax.random.split(key, 6)
        return {'x': jax.random.normal(ks[0], (BATCH, TOK, DIM), dtype=jnp.float32), 'W_base': jax.random.normal(ks[1], (OUT, DIM), dtype=jnp.float32) / np.sqrt(DIM), 'b_base': jax.random.normal(ks[2], (OUT,), dtype=jnp.float32) * 0.01, 'W_gate': jax.random.normal(ks[3], (E, DIM), dtype=jnp.float32) * 0.01, 'A': jax.random.normal(ks[4], (E, R, DIM), dtype=jnp.float32) / np.sqrt(DIM), 'B': jax.random.normal(ks[5], (OUT, OUT // OUT * R * 0 + R), dtype=jnp.float32)[None].repeat(E, 0) * 0.0 + jax.random.normal(ks[5], (E, OUT, R), dtype=jnp.float32) * 0.02}
    _L0_ffn_all = _L0_ffn_setup()
    _L0_ffn_in = {k: v for k, v in _L0_ffn_all.items() if k in ('W_base', 'b_base', 'W_gate', 'A', 'B')}
    del _L0_ffn_all

    def _L1_cond_setup():
        import jax, jax.numpy as jnp
        import numpy as np
        MAX_LORAS, OUT, IN = (8, 1024, 1024)
        B, S = (4, 512)
        key = jax.random.key(seed)
        k1, k2, k3 = jax.random.split(key, 3)
        x = jax.random.normal(k1, (B, S, IN), dtype=jnp.float32)
        weight = jax.random.normal(k2, (MAX_LORAS, OUT, IN), dtype=jnp.float32) * 0.02
        adapter_ids = jax.random.randint(k3, (B,), 0, MAX_LORAS, dtype=jnp.int32)
        return {'x': x, 'weight': weight, 'adapter_ids': adapter_ids}
    _L1_cond_all = _L1_cond_setup()
    _L1_cond_in = {k: v for k, v in _L1_cond_all.items() if k in ('weight',)}
    del _L1_cond_all

    def _L1_ffn_setup():
        import jax, jax.numpy as jnp
        import numpy as np
        ALPHA = 32
        R = 16
        SCALING = ALPHA / R
        key = jax.random.key(seed)
        k1, k2, k3, k4 = jax.random.split(key, 4)
        B_, S, D = (4, 512, 1024)
        H, r, O = (8, R, 1024)
        x = jax.random.normal(k1, (B_, S, D), dtype=jnp.float32)
        A = jax.random.normal(k2, (H, r, D), dtype=jnp.float32) * 0.02
        Bm = jax.random.normal(k3, (H, O, r), dtype=jnp.float32) * 0.02
        Wr = jax.random.normal(k4, (H, D), dtype=jnp.float32) * 0.02
        br = jnp.zeros((H,), dtype=jnp.float32)
        return {'x': x, 'A': A, 'B': Bm, 'Wr': Wr, 'br': br}
    _L1_ffn_all = _L1_ffn_setup()
    _L1_ffn_in = {k: v for k, v in _L1_ffn_all.items() if k in ('A', 'B', 'Wr', 'br')}
    del _L1_ffn_all
    return {'x': x, 'itok_B_0_15': itok_B_0_15, 'itok_B_3_7': itok_B_3_7, 'L0_cond_weights': _L0_cond_in['weights'], 'L0_ffn_W_base': _L0_ffn_in['W_base'], 'L0_ffn_b_base': _L0_ffn_in['b_base'], 'L0_ffn_W_gate': _L0_ffn_in['W_gate'], 'L0_ffn_A': _L0_ffn_in['A'], 'L0_ffn_B': _L0_ffn_in['B'], 'L1_cond_weight': _L1_cond_in['weight'], 'L1_ffn_A': _L1_ffn_in['A'], 'L1_ffn_B': _L1_ffn_in['B'], 'L1_ffn_Wr': _L1_ffn_in['Wr'], 'L1_ffn_br': _L1_ffn_in['br']}

def reference(x, itok_B_0_15, itok_B_3_7, L0_cond_weights, L0_ffn_W_base, L0_ffn_b_base, L0_ffn_W_gate, L0_ffn_A, L0_ffn_B, L1_cond_weight, L1_ffn_A, L1_ffn_B, L1_ffn_Wr, L1_ffn_br):
    import jax
    import jax.numpy as jnp

    def _L0_cond_ref(x, weights, condition):
        import jax, jax.numpy as jnp
        import numpy as np
        NUM_CONDITIONS = 16
        IN_CH = 64
        OUT_CH = 64
        B = 64
        T = 1024
        W = weights[condition]
        return jnp.einsum('bct,bcd->bdt', x, W)

    def _L0_ffn_ref(x, W_base, b_base, W_gate, A, B):
        import jax, jax.numpy as jnp
        import numpy as np
        BATCH, TOK, DIM, OUT = (4, 512, 1024, 1024)
        E, R, TOP_K = (8, 16, 2)
        SCALING = 16.0 / R
        result = jnp.einsum('bnd,od->bno', x, W_base) + b_base
        logits = jnp.einsum('bnd,ed->bne', x, W_gate)
        probs = jax.nn.softmax(logits.astype(jnp.float32), axis=-1)
        top_p, top_i = jax.lax.top_k(probs, TOP_K)
        top_p = top_p / jnp.sum(top_p, axis=-1, keepdims=True)
        top_p = top_p.astype(x.dtype)
        route_w = jnp.sum(jax.nn.one_hot(top_i, E, dtype=x.dtype) * top_p[..., None], axis=-2)
        h = jnp.einsum('bnd,erd->bner', x, A)
        hw = h * route_w[..., None]
        delta = jnp.einsum('bner,eor->bno', hw, B)
        return result + delta * SCALING

    def _L1_cond_ref(x, weight, adapter_ids):
        import jax, jax.numpy as jnp
        import numpy as np
        MAX_LORAS, OUT, IN = (8, 1024, 1024)
        B, S = (4, 512)
        w = weight[adapter_ids]
        return jnp.einsum('bsi,boi->bso', x, w)

    def _L1_ffn_ref(x, A, B, Wr, br):
        import jax, jax.numpy as jnp
        import numpy as np
        ALPHA = 32
        R = 16
        SCALING = ALPHA / R
        H = A.shape[0]
        router_logits = jnp.einsum('bsd,hd->bsh', x, Wr) + br
        scores = H * jax.nn.softmax(router_logits, axis=-1)
        low = jnp.einsum('bsd,hrd->bshr', x, A)
        out = jnp.einsum('bshr,hor,bsh->bso', low, B, scores)
        return SCALING * out
    x = x + _L0_ffn_ref(_L0_cond_ref(x, L0_cond_weights, itok_B_0_15), L0_ffn_W_base, L0_ffn_b_base, L0_ffn_W_gate, L0_ffn_A, L0_ffn_B)
    x = x + _L1_ffn_ref(_L1_cond_ref(x, L1_cond_weight, itok_B_3_7), L1_ffn_A, L1_ffn_B, L1_ffn_Wr, L1_ffn_br)
    return x

_drawn_inputs = setup_inputs


def setup_inputs(seed=0):
    import zlib

    import numpy as np

    out = dict(_drawn_inputs(seed))
    spreads = {'L1_ffn_br': (0.0, 0.542)}
    factors = {'L0_ffn_b_base': 8.0}
    for name, (base, spread) in spreads.items():
        noise = np.random.default_rng([zlib.crc32(name.encode()), seed]).standard_normal(out[name].shape)
        drawn = base * np.exp(spread * noise) if base else spread * noise
        out[name] = jnp.asarray(drawn.astype(out[name].dtype))
    for name, factor in factors.items():
        out[name] = (out[name] * factor).astype(out[name].dtype)
    return out
```

```python
from contextlib import ExitStack

import concourse.bass as bass
from concourse import mybir

F32 = mybir.dt.float32
F32R = mybir.dt.float32r
I32 = mybir.dt.int32
U32 = mybir.dt.uint32
ALU = mybir.AluOpType
ACT = mybir.ActivationFunctionType
AX = mybir.AxisListType

P = 128
SAMPLES = 64
CH = 64
D = 1024
KC = D // P
TILES = SAMPLES * CH // P
CONDS = 16
EXPERTS = 8
RANK = 16
HR = EXPERTS * RANK
HG = HR + EXPERTS
NW = HG + D
GROUPS = [(0, 386), (386, 774), (774, NW)]
L1_SCALE = 16.0
RING = 4
UNITS = EXPERTS * KC
FIRST_UNIT = 4
W0_PIECE = KC * NW // 10
W0_PIECES = 10


def build(nc, x, cond_ids, adapter_ids, w_cond, w0, bias, b0, w1, ag1, b1, br, out):
    with ExitStack() as ctx:
        def sb(name, shape, dt):
            return ctx.enter_context(nc.sbuf_tensor(name, shape, dt))

        def ps(name):
            return ctx.enter_context(nc.psum_tensor(name, [P, 512], F32))

        def sem(name):
            return ctx.enter_context(nc.semaphore(name))

        w0_hi = sb("w0_hi", [P, KC * NW], F32R)
        w0_lo = sb("w0_lo", [P, KC * NW], F32R)
        b0_hi = sb("b0_hi", [P, D], F32R)
        b0_lo = sb("b0_lo", [P, D], F32R)
        b1_hi = sb("b1_hi", [P, D], F32R)
        b1_lo = sb("b1_lo", [P, D], F32R)
        folded = sb("folded", [P, EXPERTS, KC, HG], F32)
        cond_table = sb("cond_table", [P, CONDS, CH], F32)
        bias_rows = sb("bias_rows", [P, D], F32)
        br_rows = sb("br_rows", [P, EXPERTS], F32)
        ids = sb("ids", [1, 2 * SAMPLES], I32)
        identity = sb("identity", [P, P], F32)
        expert_no = sb("expert_no", [P, EXPERTS], F32)

        ring = sb("ring", [P, RING, D], F32)
        yT = sb("yT", [P, 2, 2, D], F32R)
        adapter_hi = sb("adapter_hi", [P, KC, 2, HG], F32R)
        adapter_lo = sb("adapter_lo", [P, KC, 2, HG], F32R)
        ag1_hi = adapter_hi[:, 0:KC // 2, :, :].rearrange("p a b n -> p (a b) n")
        ag1_lo = adapter_lo[:, 0:KC // 2, :, :].rearrange("p a b n -> p (a b) n")
        x_hi = sb("x_hi", [P, D], F32R)
        x_lo = sb("x_lo", [P, D], F32R)
        zero_cols = sb("zero_cols", [P, 1], F32)
        wait_col = sb("wait_col", [P, 1], F32)
        wc_hi = sb("wc_hi", [P, P], F32R)
        wc_lo = sb("wc_lo", [P, P], F32R)
        x1T_hi = sb("x1T_hi", [P, D], F32R)
        x1T_lo = sb("x1T_lo", [P, D], F32R)

        hg = sb("hg", [P, HG], F32)
        max0 = sb("max0", [P, 1], F32)
        top8 = sb("top8", [P, 8], F32)
        top_at = sb("top_at", [P, 8], U32)
        top_no = sb("top_no", [P, 2], F32)
        neg_max0 = sb("neg_max0", [P, 1], F32)
        top_exp = sb("top_exp", [P, 2], F32)
        top_sum = sb("top_sum", [P, 1], F32)
        top_inv = sb("top_inv", [P, 1], F32)
        top_w = sb("top_w", [P, 2], F32)
        route_a = sb("route_a", [P, EXPERTS], F32)
        route_b = sb("route_b", [P, EXPERTS], F32)
        route = sb("route", [P, EXPERTS], F32)
        hw = sb("hw", [P, HR], F32)
        hwT_hi = sb("hwT_hi", [P, P], F32R)
        hwT_lo = sb("hwT_lo", [P, P], F32R)
        lg = sb("lg", [P, HG], F32)
        logits1 = sb("logits1", [P, EXPERTS], F32)
        max1 = sb("max1", [P, 1], F32)
        neg_max1 = sb("neg_max1", [P, 1], F32)
        exp1 = sb("exp1", [P, EXPERTS], F32)
        sum1 = sb("sum1", [P, 1], F32)
        inv1 = sb("inv1", [P, 1], F32)
        score = sb("score", [P, EXPERTS], F32)
        lw = sb("lw", [P, HR], F32)
        lwT_hi = sb("lwT_hi", [P, P], F32R)
        lwT_lo = sb("lwT_lo", [P, P], F32R)

        main_ps = [ps(f"main_ps{g}") for g in range(3)]
        turn_ps = [ps(f"turn_ps{b}") for b in range(2)]
        out_ps = [ps(f"out_ps{b}") for b in range(2)]
        low_ps = ps("low_ps")

        piece_landed = [sem(f"piece_landed{s}") for s in range(RING)]
        small_landed = sem("small_landed")
        piece_hi = sem("piece_hi")
        piece_lo = sem("piece_lo")
        unit_done = sem("unit_done")
        unit_copied = sem("unit_copied")
        const_set = sem("const_set")
        x_landed = [sem(f"x_landed{s}") for s in range(RING)]
        stored = [sem(f"stored{s}") for s in range(RING)]
        x_hi_done = sem("x_hi_done")
        x_lo_done = sem("x_lo_done")
        wc_hi_done = sem("wc_hi_done")
        wc_lo_done = sem("wc_lo_done")
        xb_done = sem("xb_done")
        yT_done = sem("yT_done")
        yT_hi_done = sem("yT_hi_done")
        yT_lo_done = sem("yT_lo_done")
        hg_done = sem("hg_done")
        hg_copied = sem("hg_copied")
        route_step = sem("route_step")
        top_exp_done = sem("top_exp_done")
        hwT_done = sem("hwT_done")
        hwT_hi_done = sem("hwT_hi_done")
        hwT_lo_done = sem("hwT_lo_done")
        main_done = sem("main_done")
        x1_done = sem("x1_done")
        x1T_done = sem("x1T_done")
        x1T_hi_done = sem("x1T_hi_done")
        x1T_lo_done = sem("x1T_lo_done")
        adapter_hi_done = sem("adapter_hi_done")
        adapter_lo_done = sem("adapter_lo_done")
        low_done = sem("low_done")
        lg_copied = sem("lg_copied")
        score_step = sem("score_step")
        exp1_done = sem("exp1_done")
        lwT_done = sem("lwT_done")
        lwT_hi_done = sem("lwT_hi_done")
        lwT_lo_done = sem("lwT_lo_done")
        out_done = sem("out_done")
        final_done = sem("final_done")
        ROUTE_STEPS = 11
        SCORE_STEPS = 7

        ag1_hi_flat = ag1_hi.rearrange("p a n -> p (a n)")
        ag1_lo_flat = ag1_lo.rearrange("p a n -> p (a n)")
        HALF_AG1 = KC * HG // 2
        head_pieces = [
            (HALF_AG1, ag1[:, 0:HALF_AG1], ag1_hi_flat[:, 0:HALF_AG1], ag1_lo_flat[:, 0:HALF_AG1]),
            (HALF_AG1, ag1[:, HALF_AG1:], ag1_hi_flat[:, HALF_AG1:], ag1_lo_flat[:, HALF_AG1:]),
            (D, b0, b0_hi[:, :], b0_lo[:, :]),
            (D, b1, b1_hi[:, :], b1_lo[:, :]),
        ]
        tail_pieces = [
            (W0_PIECE, w0[:, n * W0_PIECE:(n + 1) * W0_PIECE],
             w0_hi[:, n * W0_PIECE:(n + 1) * W0_PIECE], w0_lo[:, n * W0_PIECE:(n + 1) * W0_PIECE])
            for n in range(W0_PIECES)]
        TAIL = FIRST_UNIT + UNITS
        PIECES = TAIL + W0_PIECES
        w0_hi3 = w0_hi[:, :].rearrange("p (k n) -> p k n", k=KC)
        w0_lo3 = w0_lo[:, :].rearrange("p (k n) -> p k n", k=KC)

        block = ctx.enter_context(nc.Block())

        @block.sync
        def _(sp):
            def stage(n, q, width, src):
                if n >= RING or not isinstance(q, int):
                    sp.wait_ge(piece_lo, 4 * q + n - RING + 1)
                sp.dma_start(ring[:, n % RING, 0:width], src).then_inc(piece_landed[n % RING], 16)

            for n, (width, src, _, _) in enumerate(head_pieces):
                stage(n, 0, width, src)
            with sp.Fori(0, UNITS // RING) as q:
                for j in range(RING):
                    stage(FIRST_UNIT + j, q, D, w1[bass.ds(4 * q + j, 1), :, :].rearrange("a p n -> (a p) n"))
            for n, (width, src, _, _) in enumerate(tail_pieces):
                stage(TAIL + n, 0, width, src)

            def load_x(q, r):
                s = r % RING
                sp.dma_start(ring[:, s, :], x[bass.ds(4 * q + r, 1), :, :].rearrange("a p n -> (a p) n")
                             ).then_inc(x_landed[s], 16)

            def store_out(q, r):
                s = r % RING
                sp.wait_ge(final_done, 8 * q + 2 * r + 2)
                sp.dma_start(out[bass.ds(4 * q + r, 1), :, :].rearrange("a p n -> (a p) n"), ring[:, s, :]
                             ).then_inc(stored[s], 16)

            sp.wait_ge(piece_lo, PIECES)
            for r in range(4):
                load_x(0, r)

            def iteration(q, r, last=False):
                store_out(q, r - 2)
                if not last:
                    sp.wait_ge(stored[(r - 2) % RING], 16 * q + 16 * ((r - 2) // RING + 1))
                    load_x(q, r + 2)

            with sp.Fori(0, (TILES - 4) // 4) as q:
                for r in range(2, 6):
                    iteration(q, r)
            for r in range(TILES - 2, TILES + 2):
                iteration(0, r, last=True)
            for s in range(RING):
                sp.wait_ge(stored[s], 16 * TILES // RING)

        @block.tensor
        def _(pe):
            def product(dst, st_hi, st_lo, mv_hi, mv_lo, start, stop):
                pe.matmul(dst, st_hi, mv_lo, start=start, stop=False, skip_group_check=True)
                pe.matmul(dst, st_lo, mv_hi, start=False, stop=False, skip_group_check=True)
                return pe.matmul(dst, st_hi, mv_hi, start=False, stop=stop, skip_group_check=True)

            def unit(q, n):
                u = n - FIRST_UNIT
                pe.wait_ge(piece_lo, 4 * q + n + 1)
                if u >= 2 or not isinstance(q, int):
                    pe.wait_ge(unit_copied, 4 * q + u - 1)
                for oc in range(KC):
                    mm = product(main_ps[u % 2][:, 0:HG],
                                 yT[:, u % 2, 0, oc * P:(oc + 1) * P], yT[:, u % 2, 1, oc * P:(oc + 1) * P],
                                 ag1_hi[:, oc, :], ag1_lo[:, oc, :], oc == 0, oc == KC - 1)
                mm.then_inc(unit_done, 1)

            for j in range(RING):
                unit(0, FIRST_UNIT + j)
            with pe.Fori(1, UNITS // RING) as q:
                for j in range(RING):
                    unit(q, FIRST_UNIT + j)
            pe.wait_ge(unit_copied, UNITS)
            pe.wait_ge(const_set, 7)

            def make_yT(q, r):
                pe.wait_ge(x_lo_done, 4 * q + r + 1)
                pe.wait_ge(wc_lo_done, 8 * q + 2 * r + 2)
                for c in range(KC):
                    if c % 4 == 0 and (r >= 2 or not isinstance(q, int)):
                        if r >= 3 or not isinstance(q, int):
                            pe.wait_ge(x1T_lo_done, 8 * q + 2 * (r - 3) + c // 4 + 1)
                    mm = product(turn_ps[c // 4][:, (c % 4) * P:(c % 4 + 1) * P],
                                 x_hi[:, c * P:(c + 1) * P], x_lo[:, c * P:(c + 1) * P],
                                 wc_hi[:, :], wc_lo[:, :], True, True)
                    if c % 4 == 3:
                        mm.then_inc(yT_done, 1)

            def make_out(q, r):
                pe.wait_ge(lwT_lo_done, 4 * q + r + 1)
                for b in range(2):
                    mm = product(out_ps[b][:, :], lwT_hi[:, :], lwT_lo[:, :],
                                 b1_hi[:, b * 512:(b + 1) * 512], b1_lo[:, b * 512:(b + 1) * 512], True, True)
                    mm.then_inc(out_done, 1)

            def main(q, r, g, k0, k1):
                a, b = GROUPS[g]
                s = r % 2
                for k in range(k0, k1):
                    mm = product(main_ps[g][:, 0:b - a],
                                 yT[:, s, 0, k * P:(k + 1) * P], yT[:, s, 1, k * P:(k + 1) * P],
                                 w0_hi3[:, k, a:b], w0_lo3[:, k, a:b], k == 0, False)
                return mm

            def delta(g):
                a, b = GROUPS[g]
                a0 = max(a, HG)
                return product(main_ps[g][:, a0 - a:b - a], hwT_hi[:, :], hwT_lo[:, :],
                               b0_hi[:, a0 - HG:b - HG], b0_lo[:, a0 - HG:b - HG], False, True)

            def turn_x1(q, r):
                pe.wait_ge(x1_done, 12 * q + 3 * r + 3)
                for c in range(KC):
                    mm = pe.transpose(turn_ps[c // 4][:, (c % 4) * P:(c % 4 + 1) * P],
                                      ring[:, r % RING, c * P:(c + 1) * P], identity[:, :])
                    if c % 4 == 3:
                        mm.then_inc(x1T_done, 1)

            def make_low(q, r):
                pe.wait_ge(adapter_lo_done, 8 * q + 2 * r + 2)
                pe.wait_ge(x1T_lo_done, 8 * q + 2 * r + 2)
                for k in range(KC):
                    mm = product(low_ps[:, 0:2 * HG], x1T_hi[:, k * P:(k + 1) * P], x1T_lo[:, k * P:(k + 1) * P],
                                 adapter_hi[:, k, :, :].rearrange("p b n -> p (b n)"),
                                 adapter_lo[:, k, :, :].rearrange("p b n -> p (b n)"), k == 0, k == KC - 1)
                mm.then_inc(low_done, 1)

            def iteration(q, r, l0=True, l1=True, l1_out=True, ahead=True):
                if ahead:
                    make_yT(q, r + 1)
                if l1_out:
                    make_out(q, r - 2)
                first = isinstance(q, int) and r == 0
                if l0:
                    pe.wait_ge(yT_lo_done, 8 * q + 2 * r + 2)
                    if not first:
                        pe.wait_ge(x1_done, 12 * q + 3 * (r - 1) + 1)
                    main(q, r, 0, 0, KC).then_inc(hg_done, 1)
                if l1:
                    if ahead:
                        pe.wait_ge(yT_lo_done, 8 * q + 2 * (r + 1) + 2)
                    turn_x1(q, r - 1)
                if l0:
                    if not first:
                        pe.wait_ge(x1_done, 12 * q + 3 * (r - 1) + 2)
                    main(q, r, 1, 0, KC)
                if l1:
                    if r >= 2 or not isinstance(q, int):
                        pe.wait_ge(lwT_lo_done, 4 * q + r - 1)
                    make_low(q, r - 1)
                if l0:
                    pe.wait_ge(route_step, ROUTE_STEPS * (4 * q + r + 1))
                    if r >= 2 or not isinstance(q, int):
                        pe.wait_ge(final_done, 8 * q + 2 * (r - 2) + 1)
                    pe.transpose(out_ps[0][:, 0:P], hw[:, :], identity[:, :]).then_inc(hwT_done, 1)
                    if not first:
                        pe.wait_ge(x1_done, 12 * q + 3 * (r - 1) + 3)
                    main(q, r, 2, 0, KC // 2)
                    pe.wait_ge(hwT_lo_done, 4 * q + r + 1)
                    delta(0)
                    delta(1).then_inc(main_done, 1)
                    main(q, r, 2, KC // 2, KC)
                if l1:
                    pe.wait_ge(score_step, SCORE_STEPS * (4 * q + r))
                    pe.transpose(low_ps[:, 0:P], lw[:, :], identity[:, :]).then_inc(lwT_done, 1)
                if l0:
                    delta(2).then_inc(main_done, 1)

            make_yT(0, 0)
            pe.wait_ge(yT_lo_done, 2)
            iteration(0, 0, l1=False, l1_out=False)
            iteration(0, 1, l1_out=False)
            with pe.Fori(0, (TILES - 4) // 4) as q:
                for r in range(2, 6):
                    iteration(q, r)
            iteration(0, TILES - 2)
            iteration(0, TILES - 1, ahead=False)
            iteration(0, TILES, l0=False, ahead=False)
            make_out(0, TILES - 1)

        @block.scalar
        def _(act):
            for half in range(2):
                act.dma_start(cond_table[half * CH:(half + 1) * CH, :, :], w_cond).then_inc(small_landed, 16)
            act.dma_start(bias_rows[:, :], bias.partition_broadcast(P)).then_inc(small_landed, 16)
            act.dma_start(br_rows[:, :], br.partition_broadcast(P)).then_inc(small_landed, 16)
            act.dma_start(ids[:, 0:SAMPLES], cond_ids).then_inc(small_landed, 16)
            act.dma_start(ids[:, SAMPLES:], adapter_ids).then_inc(small_landed, 16)

            def cut(n, q, width, hi):
                act.wait_ge(piece_landed[n % RING], 16 * q + 16 * (n // RING + 1))
                act.copy(hi, ring[:, n % RING, 0:width]).then_inc(piece_hi, 1)

            def copy_unit(q, u):
                act.wait_ge(unit_done, 4 * q + u + 1)
                act.copy(folded[:, :, :, :].rearrange("p e k n -> p (e k) n")[:, bass.ds(4 * q + u, 1), :]
                         .rearrange("p a n -> p (a n)"),
                         main_ps[u % 2][:, 0:HG]).then_inc(unit_copied, 1)

            for n, (width, _, hi, _) in enumerate(head_pieces):
                cut(n, 0, width, hi)

            def unit(q, u):
                if u >= 2 or not isinstance(q, int):
                    act.wait_ge(unit_done, 4 * q + u - 1)
                cut(FIRST_UNIT + u, q, D, yT[:, u % 2, 0, :])
                if u >= 1 or not isinstance(q, int):
                    copy_unit(q, u - 1)

            for u in range(RING):
                unit(0, u)
            with act.Fori(1, UNITS // RING) as q:
                for u in range(RING):
                    unit(q, u)
            copy_unit(0, UNITS - 1)
            for n, (width, _, hi, _) in enumerate(tail_pieces):
                cut(TAIL + n, 0, width, hi)
            act.wait_ge(small_landed, 96)

            def x_high(q, r):
                act.wait_ge(x_landed[r % RING], 16 * q + 16 * (r // RING + 1))
                if r >= 1 or not isinstance(q, int):
                    act.wait_ge(yT_done, 8 * q + 2 * r)
                act.copy(x_hi[:, :], ring[:, r % RING, :]).then_inc(x_hi_done, 1)

            def cond_high(q, r):
                if r >= 1 or not isinstance(q, int):
                    act.wait_ge(yT_done, 8 * q + 2 * r)
                for b in range(2):
                    c = act.value_load(ids[0:1, bass.ds(8 * q + 2 * r + b, 1)], min_val=0, max_val=CONDS - 1)
                    half = slice(b * CH, (b + 1) * CH)
                    act.copy(wc_hi[half, half], cond_table[half, bass.ds(c, 1), :].rearrange("p a n -> p (a n)")
                             ).then_inc(wc_hi_done, 1)

            def yT_high(q, r):
                if r >= 2 or not isinstance(q, int):
                    act.wait_ge(main_done, 8 * q + 2 * (r - 2) + 2)
                for b in range(2):
                    act.wait_ge(yT_done, 8 * q + 2 * r + b + 1)
                    act.copy(yT[:, r % 2, 0, b * 512:(b + 1) * 512], turn_ps[b][:, :]).then_inc(yT_hi_done, 1)

            def adapter_high(q, r):
                if r >= 1 or not isinstance(q, int):
                    act.wait_ge(low_done, 4 * q + r)
                for b in range(2):
                    e = act.value_load(ids[0:1, bass.ds(SAMPLES + 8 * q + 2 * r + b, 1)],
                                       min_val=0, max_val=EXPERTS - 1)
                    act.copy(adapter_hi[:, :, b, :],
                             folded[:, bass.ds(e, 1), :, :].rearrange("p a k n -> p (a k) n")
                             ).then_inc(adapter_hi_done, 1)

            def x1T_high(q, r):
                if r >= 1 or not isinstance(q, int):
                    act.wait_ge(low_done, 4 * q + r)
                for b in range(2):
                    act.wait_ge(x1T_done, 8 * q + 2 * r + b + 1)
                    act.copy(x1T_hi[:, b * 512:(b + 1) * 512], turn_ps[b][:, :]).then_inc(x1T_hi_done, 1)

            def top_exps(q, r):
                act.wait_ge(route_step, ROUTE_STEPS * (4 * q + r) + 3)
                act.activation(top_exp[:, :], top8[:, 0:2], ACT.Exp, bias=neg_max0[:, 0:1],
                               accum_out=top_sum[:, :]).then_inc(top_exp_done, 1)

            def score_exps(q, r):
                act.wait_ge(score_step, SCORE_STEPS * (4 * q + r) + 3)
                act.activation(exp1[:, :], logits1[:, :], ACT.Exp, bias=neg_max1[:, 0:1],
                               accum_out=sum1[:, :]).then_inc(exp1_done, 1)

            def hwT_high(q, r):
                act.wait_ge(hwT_done, 4 * q + r + 1)
                if r >= 1 or not isinstance(q, int):
                    act.wait_ge(main_done, 8 * q + 2 * r)
                act.copy(hwT_hi[:, :], out_ps[0][:, 0:P]).then_inc(hwT_hi_done, 1)

            def lwT_high(q, r):
                act.wait_ge(lwT_done, 4 * q + r + 1)
                if r >= 1 or not isinstance(q, int):
                    act.wait_ge(out_done, 8 * q + 2 * r)
                act.copy(lwT_hi[:, :], low_ps[:, 0:P]).then_inc(lwT_hi_done, 1)

            def iteration(q, r, l0=True, l1=True, ahead=True, ahead2=True):
                if ahead:
                    yT_high(q, r + 1)
                if l1:
                    adapter_high(q, r - 1)
                if l1:
                    x1T_high(q, r - 1)
                if l0:
                    top_exps(q, r)
                if ahead2:
                    x_high(q, r + 2)
                    cond_high(q, r + 2)
                if l0:
                    hwT_high(q, r)
                if l1:
                    score_exps(q, r - 1)
                    lwT_high(q, r - 1)

            act.wait_ge(const_set, 7)
            x_high(0, 0)
            cond_high(0, 0)
            yT_high(0, 0)
            x_high(0, 1)
            cond_high(0, 1)
            iteration(0, 0, l1=False)
            iteration(0, 1)
            with act.Fori(0, (TILES - 4) // 4) as q:
                for r in range(2, 6):
                    iteration(q, r)
            iteration(0, TILES - 2, ahead2=False)
            iteration(0, TILES - 1, ahead=False, ahead2=False)
            iteration(0, TILES, l0=False, ahead=False, ahead2=False)

        @block.vector
        def _(dve):
            for e in range(EXPERTS):
                last = dve.memset(expert_no[:, e:e + 1], float(e))
            last.then_inc(const_set, 1)

            def cut(n, q, width, hi, lo):
                dve.wait_ge(piece_hi, 4 * q + n + 1)
                dve.tensor_tensor(lo, ring[:, n % RING, 0:width], hi, ALU.subtract).then_inc(piece_lo, 1)

            for n, (width, _, hi, lo) in enumerate(head_pieces):
                cut(n, 0, width, hi, lo)
            with dve.Fori(0, UNITS // RING) as q:
                for u in range(RING):
                    cut(FIRST_UNIT + u, q, D, yT[:, u % 2, 0, :], yT[:, u % 2, 1, :])
            for n, (width, _, hi, lo) in enumerate(tail_pieces):
                cut(TAIL + n, 0, width, hi, lo)
            dve.wait_ge(small_landed, 96)
            dve.wait_ge(const_set, 7)

            def cond_low(q, r):
                for b in range(2):
                    dve.wait_ge(wc_hi_done, 8 * q + 2 * r + b + 1)
                    c = dve.value_load(ids[0:1, bass.ds(8 * q + 2 * r + b, 1)], min_val=0, max_val=CONDS - 1)
                    half = slice(b * CH, (b + 1) * CH)
                    dve.tensor_tensor(wc_lo[half, half],
                                      cond_table[half, bass.ds(c, 1), :].rearrange("p a n -> p (a n)"),
                                      wc_hi[half, half], ALU.subtract).then_inc(wc_lo_done, 1)

            def yT_low(q, r):
                for b in range(2):
                    dve.wait_ge(yT_hi_done, 8 * q + 2 * r + b + 1)
                    dve.tensor_tensor(yT[:, r % 2, 1, b * 512:(b + 1) * 512], turn_ps[b][:, :],
                                      yT[:, r % 2, 0, b * 512:(b + 1) * 512], ALU.subtract
                                      ).then_inc(yT_lo_done, 1)

            def x1T_low(q, r):
                for b in range(2):
                    dve.wait_ge(x1T_hi_done, 8 * q + 2 * r + b + 1)
                    dve.tensor_tensor(x1T_lo[:, b * 512:(b + 1) * 512], turn_ps[b][:, :],
                                      x1T_hi[:, b * 512:(b + 1) * 512], ALU.subtract
                                      ).then_inc(x1T_lo_done, 1)

            def final(q, r):
                for b in range(2):
                    row = ring[:, r % RING, b * 512:(b + 1) * 512]
                    dve.wait_ge(out_done, 8 * q + 2 * r + b + 1)
                    dve.tensor_tensor(row, row, out_ps[b][:, :], ALU.add).then_inc(final_done, 1)

            def copy_hg(q, r):
                dve.wait_ge(hg_done, 4 * q + r + 1)
                dve.tensor_copy(hg[:, :], main_ps[0][:, 0:HG]).then_inc(hg_copied, 1)

            def routing(q, r):
                def step(instruction, n):
                    instruction.then_inc(route_step, 1)

                def after(n):
                    dve.wait_ge(route_step, ROUTE_STEPS * (4 * q + r) + n)
                dve.wait_ge(hg_copied, 4 * q + r + 1)
                logits = hg[:, HR:HG]
                step(dve.reduce_max(max0[:, :], logits, AX.X), 1)
                step(dve.max(top8[:, :], logits), 2)
                after(2)
                step(dve.tensor_scalar(neg_max0[:, :], max0[:, :], -1.0, None, ALU.mult), 3)
                step(dve.max_index(top_at[:, :], top8[:, :], logits), 4)
                after(4)
                step(dve.tensor_copy(top_no[:, :], top_at[:, 0:2]), 5)
                dve.wait_ge(top_exp_done, 4 * q + r + 1)
                step(dve.reciprocal(top_inv[:, :], top_sum[:, :]), 6)
                after(6)
                step(dve.tensor_scalar(top_w[:, :], top_exp[:, :], top_inv[:, 0:1], None, ALU.mult), 7)
                after(7)
                step(dve.tensor_scalar(route_a[:, :], expert_no[:, :], top_no[:, 0:1], top_w[:, 0:1],
                                       ALU.is_equal, ALU.mult), 8)
                step(dve.tensor_scalar(route_b[:, :], expert_no[:, :], top_no[:, 1:2], top_w[:, 1:2],
                                       ALU.is_equal, ALU.mult), 9)
                after(9)
                step(dve.tensor_tensor(route[:, :], route_a[:, :], route_b[:, :], ALU.add), 10)
                after(10)
                if r >= 1 or not isinstance(q, int):
                    dve.wait_ge(hwT_done, 4 * q + r)
                step(dve.tensor_tensor(hw[:, :].rearrange("p (e k) -> p e k", k=RANK),
                                       hg[:, 0:HR].rearrange("p (e k) -> p e k", k=RANK),
                                       route[:, :].unsqueeze(2).to_broadcast([P, EXPERTS, RANK]),
                                       ALU.mult), 11)

            def copy_lg(q, r):
                dve.wait_ge(low_done, 4 * q + r + 1)
                for b in range(2):
                    half = slice(b * CH, (b + 1) * CH)
                    dve.tensor_copy(lg[half, :], low_ps[half, b * HG:(b + 1) * HG]).then_inc(lg_copied, 1)

            def scoring(q, r):
                def after(n):
                    dve.wait_ge(score_step, SCORE_STEPS * (4 * q + r) + n)
                dve.wait_ge(lg_copied, 8 * q + 2 * r + 2)
                dve.tensor_tensor(logits1[:, :], lg[:, HR:HG], br_rows[:, :], ALU.add).then_inc(score_step, 1)
                after(1)
                dve.reduce_max(max1[:, :], logits1[:, :], AX.X).then_inc(score_step, 1)
                after(2)
                dve.tensor_scalar(neg_max1[:, :], max1[:, :], -1.0, None, ALU.mult).then_inc(score_step, 1)
                dve.wait_ge(exp1_done, 4 * q + r + 1)
                dve.reciprocal(inv1[:, :], sum1[:, :]).then_inc(score_step, 1)
                after(4)
                dve.tensor_scalar(score[:, :], exp1[:, :], inv1[:, 0:1], L1_SCALE,
                                  ALU.mult, ALU.mult).then_inc(score_step, 1)
                after(5)
                if r >= 1 or not isinstance(q, int):
                    dve.wait_ge(lwT_done, 4 * q + r)
                dve.tensor_tensor(lw[:, :].rearrange("p (e k) -> p e k", k=RANK),
                                  lg[:, 0:HR].rearrange("p (e k) -> p e k", k=RANK),
                                  score[:, :].unsqueeze(2).to_broadcast([P, EXPERTS, RANK]),
                                  ALU.mult).then_inc(score_step, 2)

            def hwT_low(q, r):
                dve.wait_ge(hwT_hi_done, 4 * q + r + 1)
                dve.tensor_tensor(hwT_lo[:, :], out_ps[0][:, 0:P], hwT_hi[:, :], ALU.subtract
                                  ).then_inc(hwT_lo_done, 1)

            def lwT_low(q, r):
                dve.wait_ge(lwT_hi_done, 4 * q + r + 1)
                dve.tensor_tensor(lwT_lo[:, :], low_ps[:, 0:P], lwT_hi[:, :], ALU.subtract
                                  ).then_inc(lwT_lo_done, 1)

            def add_base(q, r, g):
                a, b = GROUPS[g]
                a0 = max(a, HG)
                row = ring[:, r % RING, a0 - HG:b - HG]
                dve.tensor_tensor(row, row, main_ps[g][:, a0 - a:b - a], ALU.add).then_inc(x1_done, 1)

            def iteration(q, r, l0=True, l1=True, l1_out=True, ahead=True, ahead2=True):
                if ahead:
                    yT_low(q, r + 1)
                if l1_out:
                    final(q, r - 2)
                if l0:
                    copy_hg(q, r)
                if l1:
                    x1T_low(q, r - 1)
                if l0:
                    routing(q, r)
                if l1:
                    copy_lg(q, r - 1)
                if ahead2:
                    cond_low(q, r + 2)
                if l0:
                    hwT_low(q, r)
                if l1:
                    scoring(q, r - 1)
                if l0:
                    dve.wait_ge(xb_done, 4 * q + r + 1)
                    dve.wait_ge(main_done, 8 * q + 2 * r + 1)
                    add_base(q, r, 0)
                    add_base(q, r, 1)
                if l1:
                    lwT_low(q, r - 1)
                if l0:
                    dve.wait_ge(main_done, 8 * q + 2 * r + 2)
                    add_base(q, r, 2)

            cond_low(0, 0)
            yT_low(0, 0)
            cond_low(0, 1)
            iteration(0, 0, l1=False, l1_out=False)
            iteration(0, 1, l1_out=False)
            with dve.Fori(0, (TILES - 4) // 4) as q:
                for r in range(2, 6):
                    iteration(q, r)
            iteration(0, TILES - 2, ahead2=False)
            iteration(0, TILES - 1, ahead=False, ahead2=False)
            iteration(0, TILES, l0=False, ahead=False, ahead2=False)
            final(0, TILES - 1)

        @block.gpsimd
        def _(pool):
            pool.memset(identity[:, :], 0.0).then_inc(const_set, 1)
            pool.memset(wc_hi[:, :].bitcast(F32), 0.0).then_inc(const_set, 1)
            pool.memset(wc_lo[:, :].bitcast(F32), 0.0).then_inc(const_set, 1)
            pool.memset(zero_cols[:, :], 0.0).then_inc(const_set, 1)
            pool.wait_ge(const_set, 5)
            pool.affine_select(out=identity[:, :], in_=identity[:, :], compare_op=ALU.not_equal, fill=1.0,
                               base=0, pattern=[[-1, P]], channel_multiplier=1).then_inc(const_set, 2)
            pool.wait_ge(small_landed, 96)

            def x_low(q, r):
                pool.wait_ge(x_hi_done, 4 * q + r + 1)
                row = ring[:, r % RING, :]
                pool.tensor_tensor(x_lo[:, :], row, x_hi[:, :], ALU.subtract).then_inc(x_lo_done, 1)
                pool.wait_ge(x_lo_done, 4 * q + r + 1)
                pool.tensor_tensor(row, row, bias_rows[:, :], ALU.add).then_inc(xb_done, 1)

            def adapter_low(q, r):
                if r >= 1 or not isinstance(q, int):
                    pool.wait_ge(adapter_lo_done, 8 * q + 2 * r)
                pool.wait_ge(adapter_hi_done, 8 * q + 2 * r + 2)
                pool.tensor_tensor(wait_col[:, :], zero_cols[:, :], zero_cols[:, :], ALU.add)
                for b in range(2):
                    e = pool.value_load(ids[0:1, bass.ds(SAMPLES + 8 * q + 2 * r + b, 1)],
                                        min_val=0, max_val=EXPERTS - 1)
                    pool.tensor_tensor(adapter_lo[:, :, b, :],
                                       folded[:, bass.ds(e, 1), :, :].rearrange("p a k n -> p (a k) n"),
                                       adapter_hi[:, :, b, :], ALU.subtract).then_inc(adapter_lo_done, 1)

            def iteration(q, r, l1=True, ahead2=True):
                if l1:
                    adapter_low(q, r - 1)
                if ahead2:
                    x_low(q, r + 2)

            for r in range(2):
                x_low(0, r)
            iteration(0, 0, l1=False)
            iteration(0, 1)
            with pool.Fori(0, (TILES - 4) // 4) as q:
                for r in range(2, 6):
                    iteration(q, r)
            for r in range(TILES - 2, TILES + 1):
                iteration(0, r, ahead2=False)


def kernel(**inputs):
    import numpy as np
    import concourse.bacc as bacc
    from concourse.bass_utils import run_bass_kernel_spmd

    def get(name):
        return np.asarray(inputs[name])

    def chunked(a, columns):
        return a.reshape(KC, P, columns).transpose(1, 0, 2).reshape(P, KC * columns)

    w0 = np.concatenate([get("L0_ffn_A").reshape(HR, D), get("L0_ffn_W_gate"), get("L0_ffn_W_base")], axis=0)
    ag1 = np.concatenate([get("L1_ffn_A").reshape(HR, D), get("L1_ffn_Wr")], axis=0)
    w1 = get("L1_cond_weight").reshape(EXPERTS, KC, P, KC, P).transpose(0, 3, 2, 1, 4).reshape(UNITS, P, D)
    arrays = {
        "x": get("x").reshape(TILES, P, D),
        "cond_ids": get("itok_B_0_15").reshape(1, SAMPLES),
        "adapter_ids": get("itok_B_3_7").reshape(1, SAMPLES),
        "w_cond": get("L0_cond_weights").transpose(1, 0, 2),
        "w0": chunked(w0.T, NW),
        "bias": get("L0_ffn_b_base"),
        "b0": get("L0_ffn_B").transpose(0, 2, 1).reshape(HR, D),
        "w1": w1,
        "ag1": chunked(ag1.T, HG),
        "b1": get("L1_ffn_B").transpose(0, 2, 1).reshape(HR, D),
        "br": get("L1_ffn_br"),
    }
    nc = bacc.Bacc("TRN2", target_bir_lowering=False, num_devices=1)
    args = []
    feed = {}
    for name, a in arrays.items():
        a = np.ascontiguousarray(a)
        feed["in_" + name] = a
        args.append(nc.dram_tensor("in_" + name, a.shape, mybir.dt.from_np(a.dtype), kind="ExternalInput").ap())
    out = nc.dram_tensor("out", (TILES, P, D), F32, kind="ExternalOutput").ap()
    build(nc, *args, out)
    result = run_bass_kernel_spmd(nc, [feed], core_ids=[0])
    return result.results[0]["out"].reshape(SAMPLES, CH, D)
```

```python
from contextlib import ExitStack

import concourse.bass as bass
from concourse import mybir

F32 = mybir.dt.float32
F32R = mybir.dt.float32r
I32 = mybir.dt.int32
U32 = mybir.dt.uint32
ALU = mybir.AluOpType
ACT = mybir.ActivationFunctionType
AX = mybir.AxisListType

P = 128
SAMPLES = 64
CH = 64
D = 1024
KC = D // P
TILES = SAMPLES * CH // P
CONDS = 16
EXPERTS = 8
RANK = 16
HR = EXPERTS * RANK
HG = HR + EXPERTS
NW = HG + D
GROUPS = [(0, 386), (386, 774), (774, NW)]
L1_SCALE = 16.0
RING = 4
UNITS = EXPERTS * KC
W0_PIECES = 10
W0_PIECE = KC * NW // W0_PIECES
TURN_AT = 3
BANKS = 2


def build(nc, x, cond_ids, adapter_ids, w_cond, w0, bias, b0, w1, ag1, b1, br, out):
    with ExitStack() as ctx:
        def sb(name, shape, dt):
            return ctx.enter_context(nc.sbuf_tensor(name, shape, dt))

        def ps(name):
            return ctx.enter_context(nc.psum_tensor(name, [P, 512], F32))

        def sem(name):
            return ctx.enter_context(nc.semaphore(name))

        w0_hi = sb("w0_hi", [P, KC * NW], F32R)
        w0_lo = sb("w0_lo", [P, KC * NW], F32R)
        b0_hi = sb("b0_hi", [P, D], F32R)
        b0_lo = sb("b0_lo", [P, D], F32R)
        b1_hi = sb("b1_hi", [P, D], F32R)
        b1_lo = sb("b1_lo", [P, D], F32R)
        folded = sb("folded", [P, EXPERTS, KC, HG], F32)
        cond_table = sb("cond_table", [P, CONDS, CH], F32)
        bias_rows = sb("bias_rows", [P, D], F32)
        br_rows = sb("br_rows", [P, EXPERTS], F32)
        ids = sb("ids", [1, 2 * SAMPLES], I32)
        identity = sb("identity", [P, P], F32)
        expert_no = sb("expert_no", [P, EXPERTS], F32)

        ring = sb("ring", [P, RING, D], F32)
        yT = sb("yT", [P, 2, 2, D], F32R)
        adapter = sb("adapter", [P, KC, 2, 2, HG], F32R)
        ag1_cut = adapter[:, :, 0, :, :]
        x_hi = sb("x_hi", [P, D], F32R)
        x_lo = sb("x_lo", [P, D], F32R)
        zero_cols = sb("zero_cols", [P, 1], F32)
        wait_col = sb("wait_col", [P, 1], F32)
        wc_raw = sb("wc_raw", [P, CH], F32)
        wc = sb("wc", [P, 2, P], F32R)
        y32 = sb("y32", [P, D], F32)
        x1T = sb("x1T", [P, KC, 2, 2, CH], F32R)

        scratch = folded[0:1, 0, :, :].rearrange("p k n -> p (k n)")
        EE = EXPERTS * EXPERTS
        asks = scratch[:, 0:EXPERTS * SAMPLES].rearrange("p (e s) -> p e s", e=EXPERTS)
        lower = scratch[:, 512:512 + EE].rearrange("p (e j) -> p e j", e=EXPERTS)
        pairs = scratch[:, 576:576 + EE].rearrange("p (j e) -> p j e", j=EXPERTS)
        ids_f = scratch[:, 640:640 + SAMPLES]
        used = scratch[:, 704:712]
        used_before = scratch[:, 712:720]
        used_no = scratch[:, 720:728]
        plan_f = scratch[:, 728:737]
        plan = sb("plan", [1, EXPERTS + 1], I32)

        hg = sb("hg", [P, HG], F32)
        max0 = sb("max0", [P, 1], F32)
        top8 = sb("top8", [P, 8], F32)
        top_at = sb("top_at", [P, 8], U32)
        top_no = sb("top_no", [P, 2], F32)
        neg_max0 = sb("neg_max0", [P, 1], F32)
        top_exp = sb("top_exp", [P, 2], F32)
        top_sum = sb("top_sum", [P, 1], F32)
        top_inv = sb("top_inv", [P, 1], F32)
        top_w = sb("top_w", [P, 2], F32)
        route_a = sb("route_a", [P, EXPERTS], F32)
        route_b = sb("route_b", [P, EXPERTS], F32)
        route = sb("route", [P, EXPERTS], F32)
        hw = sb("hw", [P, HR], F32)
        hwT_hi = sb("hwT_hi", [P, P], F32R)
        hwT_lo = sb("hwT_lo", [P, P], F32R)
        low_hi = sb("low_hi", [P, HG], F32)
        low_lo = sb("low_lo", [P, HG], F32)
        lg = sb("lg", [P, HG], F32)
        logits1 = sb("logits1", [P, EXPERTS], F32)
        max1 = sb("max1", [P, 1], F32)
        neg_max1 = sb("neg_max1", [P, 1], F32)
        exp1 = sb("exp1", [P, EXPERTS], F32)
        sum1 = sb("sum1", [P, 1], F32)
        inv1 = sb("inv1", [P, 1], F32)
        score = sb("score", [P, EXPERTS], F32)
        lw = sb("lw", [P, HR], F32)
        lwT_hi = sb("lwT_hi", [P, P], F32R)
        lwT_lo = sb("lwT_lo", [P, P], F32R)

        main_ps = [ps(f"main_ps{g}") for g in range(3)]
        turn_ps = [ps(f"turn_ps{b}") for b in range(2)]
        out_ps = [ps(f"out_ps{b}") for b in range(2)]
        low_ps = ps("low_ps")

        ag1_landed = sem("ag1_landed")
        ids_landed = sem("ids_landed")
        small_landed = sem("small_landed")
        bias_landed = sem("bias_landed")
        plan_step = sem("plan_step")
        unit_landed = [sem(f"unit_landed{s}") for s in range(RING)]
        side_landed = [sem(f"side_landed{s}") for s in range(2)]
        ag1_hi_done = sem("ag1_hi_done")
        ag1_lo_done = sem("ag1_lo_done")
        unit_hi = sem("unit_hi")
        unit_lo = sem("unit_lo")
        unit_done = sem("unit_done")
        unit_copied = sem("unit_copied")
        side_hi = sem("side_hi")
        side_lo = sem("side_lo")
        const_set = sem("const_set")
        expert_no_set = sem("expert_no_set")
        x_landed = [sem(f"x_landed{s}") for s in range(RING)]
        stored = [sem(f"stored{s}") for s in range(RING)]
        x_hi_done = sem("x_hi_done")
        x_lo_done = sem("x_lo_done")
        wc_raw_done = sem("wc_raw_done")
        wc_hi_done = sem("wc_hi_done")
        wc_lo_done = sem("wc_lo_done")
        xb_done = sem("xb_done")
        yT_done = sem("yT_done")
        y_summed = sem("y_summed")
        yT_hi_done = sem("yT_hi_done")
        yT_lo_done = sem("yT_lo_done")
        hg_done = sem("hg_done")
        hg_copied = sem("hg_copied")
        route_step = sem("route_step")
        top_exp_done = sem("top_exp_done")
        hwT_done = sem("hwT_done")
        hwT_hi_done = sem("hwT_hi_done")
        hwT_lo_done = sem("hwT_lo_done")
        main_done = sem("main_done")
        x1_done = sem("x1_done")
        x1T_done = sem("x1T_done")
        x1T_hi_done = sem("x1T_hi_done")
        x1T_lo_done = sem("x1T_lo_done")
        adapter_hi_done = sem("adapter_hi_done")
        adapter_lo_done = sem("adapter_lo_done")
        low_done = sem("low_done")
        halves_summed = sem("halves_summed")
        lg_done = sem("lg_done")
        score_step = sem("score_step")
        exp1_done = sem("exp1_done")
        lwT_done = sem("lwT_done")
        lwT_hi_done = sem("lwT_hi_done")
        lwT_lo_done = sem("lwT_lo_done")
        out_done = sem("out_done")
        final_done = sem("final_done")
        PLAN_STEPS = 11
        ROUTE_STEPS = 11
        SCORE_STEPS = 7

        ag1_raw = folded[:, EXPERTS - 1, :, :]
        side_raw = [y32, bias_rows]
        sides = [(W0_PIECE, w0[:, n * W0_PIECE:(n + 1) * W0_PIECE],
                  w0_hi[:, n * W0_PIECE:(n + 1) * W0_PIECE], w0_lo[:, n * W0_PIECE:(n + 1) * W0_PIECE])
                 for n in range(W0_PIECES)]
        sides += [(D, b0, b0_hi[:, :], b0_lo[:, :]), (D, b1, b1_hi[:, :], b1_lo[:, :])]

        def adapters_in_use(eng):
            eng.wait_ge(plan_step, PLAN_STEPS)
            return eng.value_load(plan[0:1, EXPERTS:EXPERTS + 1], min_val=1, max_val=EXPERTS)

        def adapter_at(eng, n):
            return eng.value_load(plan[0:1, bass.ds(n, 1)], min_val=0, max_val=EXPERTS - 1)

        x1T_flat = x1T[:, :, :, :, :].rearrange("p k s h t -> p (k s h t)")
        unit_cut = [(yT[:, 0, 0, :], yT[:, 0, 1, :]), (yT[:, 1, 0, :], yT[:, 1, 1, :]),
                    (x_hi[:, :], x_lo[:, :]), (x1T_flat[:, 0:D], x1T_flat[:, D:2 * D])]

        w0_hi3 = w0_hi[:, :].rearrange("p (k n) -> p k n", k=KC)
        w0_lo3 = w0_lo[:, :].rearrange("p (k n) -> p k n", k=KC)

        def turned(b):
            return turn_ps[b][:, :].rearrange("p (k s t) -> p k s t", k=KC // 2, s=2)

        def x1T_part(b, part):
            return x1T[:, b * KC // 2:(b + 1) * KC // 2, :, part, :]

        block = ctx.enter_context(nc.Block())

        @block.sync
        def _(sp):
            sp.dma_start(ids[:, SAMPLES:], adapter_ids).then_inc(ids_landed, 16)
            sp.dma_start(ag1_raw.rearrange("p k n -> p (k n)"), ag1).then_inc(ag1_landed, 16)
            in_use = adapters_in_use(sp)
            with sp.Fori(0, in_use) as n:
                e = adapter_at(sp, n)
                for c in range(KC):
                    sp.wait_ge(unit_lo, KC * n + c + 1)
                    sp.dma_start(ring[:, c % RING, :], w1[bass.ds(KC * e + c, 1), :, :].rearrange("a p n -> (a p) n")
                                 ).then_inc(unit_landed[c % RING], 16)

            def load_x(q, r):
                s = r % RING
                sp.dma_start(ring[:, s, :], x[bass.ds(4 * q + r, 1), :, :].rearrange("a p n -> (a p) n")
                             ).then_inc(x_landed[s], 16)

            def store_out(q, r):
                s = r % RING
                sp.wait_ge(final_done, 8 * q + 2 * r + 2)
                sp.dma_start(out[bass.ds(4 * q + r, 1), :, :].rearrange("a p n -> (a p) n"), ring[:, s, :]
                             ).then_inc(stored[s], 16)

            for r in range(RING):
                sp.wait_ge(unit_lo, KC * in_use + r + 1)
                load_x(0, r)

            def iteration(q, r, last=False):
                store_out(q, r - 2)
                if not last:
                    sp.wait_ge(stored[(r - 2) % RING], 16 * q + 16 * ((r - 2) // RING + 1))
                    load_x(q, r + 2)

            with sp.Fori(0, (TILES - 4) // 4) as q:
                for r in range(2, 6):
                    iteration(q, r)
            for r in range(TILES - 2, TILES + 2):
                iteration(0, r, last=True)
            for s in range(RING):
                sp.wait_ge(stored[s], 16 * TILES // RING)

        @block.tensor
        def _(pe):
            def product(dst, st_hi, st_lo, mv_hi, mv_lo, start, stop):
                pe.matmul(dst, st_hi, mv_lo, start=start, stop=False, skip_group_check=True)
                pe.matmul(dst, st_lo, mv_hi, start=False, stop=False, skip_group_check=True)
                return pe.matmul(dst, st_hi, mv_hi, start=False, stop=stop, skip_group_check=True)

            in_use = adapters_in_use(pe)
            pe.wait_ge(ag1_lo_done, 1)
            with pe.Fori(0, in_use) as n:
                for c in range(KC):
                    pe.wait_ge(unit_lo, KC * n + c + 1 + RING)
                    pe.wait_ge(unit_copied, KC * n + c + 1)
                    for oc in range(KC):
                        for part in range(2):
                            mm = pe.matmul(main_ps[c % BANKS][:, 0:2 * HG],
                                           unit_cut[c % RING][part][:, oc * P:(oc + 1) * P],
                                           ag1_cut[:, oc, :, :].rearrange("p h n -> p (h n)"),
                                           start=(oc == 0 and part == 0), stop=(oc == KC - 1 and part == 1))
                    mm.then_inc(unit_done, 1)
            pe.wait_ge(unit_copied, KC * in_use + BANKS)
            pe.wait_ge(side_lo, len(sides))
            pe.wait_ge(const_set, 6)

            def make_yT(q, r, batch):
                later = not isinstance(q, int)
                if batch == 0:
                    pe.wait_ge(x_lo_done, 4 * q + r + 1)
                    pe.wait_ge(wc_lo_done, 8 * q + 2 * r + 2)
                    if r >= 3 or later:
                        pe.wait_ge(lg_done, 8 * q + 2 * (r - 3) + 2)
                for c in range(batch * KC // 2, (batch + 1) * KC // 2):
                    if batch == 1 and c % 2 == 0:
                        pe.wait_ge(y_summed, 16 * q + 4 * r + c // 2 - 1)
                    bank = turn_ps[c // 2 % 2]
                    at = c % 2 * 2 * P
                    pe.matmul(bank[:, at:at + 2 * P], x_hi[:, c * P:(c + 1) * P],
                              wc[:, :, :].rearrange("p h n -> p (h n)"),
                              start=True, stop=False, skip_group_check=True)
                    mm = pe.matmul(bank[:, at:at + P], x_lo[:, c * P:(c + 1) * P], wc[:, 0, :],
                                   start=False, stop=True, skip_group_check=True)
                    if c % 2 == 1:
                        mm.then_inc(yT_done, 1)

            def make_out(q, r):
                pe.wait_ge(lwT_lo_done, 4 * q + r + 1)
                for b in range(2):
                    mm = product(out_ps[b][:, :], lwT_hi[:, :], lwT_lo[:, :],
                                 b1_hi[:, b * 512:(b + 1) * 512], b1_lo[:, b * 512:(b + 1) * 512], True, True)
                    mm.then_inc(out_done, 1)

            def main(q, r, g, k0, k1):
                a, b = GROUPS[g]
                s = r % 2
                for k in range(k0, k1):
                    mm = product(main_ps[g][:, 0:b - a],
                                 yT[:, s, 0, k * P:(k + 1) * P], yT[:, s, 1, k * P:(k + 1) * P],
                                 w0_hi3[:, k, a:b], w0_lo3[:, k, a:b], k == 0, False)
                return mm

            def delta(g):
                a, b = GROUPS[g]
                a0 = max(a, HG)
                return product(main_ps[g][:, a0 - a:b - a], hwT_hi[:, :], hwT_lo[:, :],
                               b0_hi[:, a0 - HG:b - HG], b0_lo[:, a0 - HG:b - HG], False, True)

            def turn_x1(q, r):
                pe.wait_ge(x1_done, 12 * q + 3 * r + 3)
                for c in range(KC):
                    mm = pe.transpose(turn_ps[c // 4][:, (c % 4) * P:(c % 4 + 1) * P],
                                      ring[:, r % RING, c * P:(c + 1) * P], identity[:, :])
                    if c % 4 == 3:
                        mm.then_inc(x1T_done, 1)

            def make_low(q, r):
                pe.wait_ge(adapter_lo_done, 8 * q + 2 * r + 2)
                pe.wait_ge(x1T_lo_done, 8 * q + 2 * r + 2)
                for b, bank in enumerate((low_ps, turn_ps[0])):
                    for k in range(KC):
                        mm = pe.matmul(bank[:, 0:2 * HG], x1T[:, k, b, :, :].rearrange("p h n -> p (h n)"),
                                       adapter[:, k, b, :, :].rearrange("p h n -> p (h n)"),
                                       start=(k == 0), stop=(k == KC - 1))
                    mm.then_inc(low_done, 1)

            def iteration(q, r, l0=True, l1=True, l1_out=True, ahead=True):
                if l1_out:
                    make_out(q, r - 2)
                if ahead:
                    make_yT(q, r + 1, 0)
                first = isinstance(q, int) and r == 0
                if l0:
                    pe.wait_ge(yT_lo_done, 8 * q + 2 * r + 2)
                    if not first:
                        pe.wait_ge(x1_done, 12 * q + 3 * (r - 1) + 1)
                    main(q, r, 0, 0, KC).then_inc(hg_done, 1)
                if ahead:
                    make_yT(q, r + 1, 1)
                if l0:
                    if not first:
                        pe.wait_ge(x1_done, 12 * q + 3 * (r - 1) + 2)
                    main(q, r, 1, 0, TURN_AT)
                if l1:
                    if ahead:
                        pe.wait_ge(y_summed, 16 * q + 4 * (r + 1) + 4)
                    turn_x1(q, r - 1)
                if l0:
                    main(q, r, 1, TURN_AT, KC)
                if l1:
                    if r >= 2 or not isinstance(q, int):
                        pe.wait_ge(lwT_lo_done, 4 * q + r - 1)
                    make_low(q, r - 1)
                if l0:
                    pe.wait_ge(route_step, ROUTE_STEPS * (4 * q + r + 1))
                    if r >= 2 or not isinstance(q, int):
                        pe.wait_ge(final_done, 8 * q + 2 * (r - 2) + 1)
                    pe.transpose(out_ps[0][:, 0:P], hw[:, :], identity[:, :]).then_inc(hwT_done, 1)
                    if not first:
                        pe.wait_ge(x1_done, 12 * q + 3 * (r - 1) + 3)
                    main(q, r, 2, 0, KC)
                if l1:
                    pe.wait_ge(score_step, SCORE_STEPS * (4 * q + r))
                    pe.transpose(low_ps[:, 0:P], lw[:, :], identity[:, :]).then_inc(lwT_done, 1)
                if l0:
                    pe.wait_ge(hwT_lo_done, 4 * q + r + 1)
                    for g in range(3):
                        delta(g).then_inc(main_done, 1)

            make_yT(0, 0, 0)
            make_yT(0, 0, 1)
            pe.wait_ge(y_summed, 4)
            iteration(0, 0, l1=False, l1_out=False)
            iteration(0, 1, l1_out=False)
            with pe.Fori(0, (TILES - 4) // 4) as q:
                for r in range(2, 6):
                    iteration(q, r)
            iteration(0, TILES - 2)
            iteration(0, TILES - 1, ahead=False)
            iteration(0, TILES, l0=False, ahead=False)
            make_out(0, TILES - 1)

        @block.scalar
        def _(act):
            for half in range(2):
                act.dma_start(cond_table[half * CH:(half + 1) * CH, :, :], w_cond).then_inc(small_landed, 16)
            act.dma_start(br_rows[:, :], br.partition_broadcast(P)).then_inc(small_landed, 16)
            act.dma_start(ids[:, 0:SAMPLES], cond_ids).then_inc(small_landed, 16)

            act.wait_ge(ag1_landed, 16)
            act.copy(ag1_cut[:, :, 0, :], ag1_raw).then_inc(ag1_hi_done, 1)

            in_use = adapters_in_use(act)
            with act.Fori(0, in_use) as n:
                for c in range(KC):
                    act.wait_ge(unit_done, KC * n + c + 1)
                    act.wait_ge(unit_landed[c % RING], 32 * n + 16 * (c // RING + 1))
                    act.copy(unit_cut[c % RING][0], ring[:, c % RING, :]).then_inc(unit_hi, 1)
            act.wait_ge(small_landed, 64)
            act.wait_ge(ids_landed, 16)
            act.wait_ge(unit_done, KC * in_use + RING)

            def x_high(q, r):
                act.wait_ge(x_landed[r % RING], 16 * q + 16 * (r // RING + 1))
                if r >= 1 or not isinstance(q, int):
                    act.wait_ge(yT_done, 16 * q + 4 * r)
                act.copy(x_hi[:, :], ring[:, r % RING, :]).then_inc(x_hi_done, 1)

            def cond_nos(q, r):
                return [act.value_load(ids[0:1, bass.ds(8 * q + 2 * r + b, 1)], min_val=0, max_val=CONDS - 1)
                        for b in range(2)]

            def cond_high(q, r, nos):
                if r >= 1 or not isinstance(q, int):
                    act.wait_ge(yT_done, 16 * q + 4 * r)
                    act.wait_ge(wc_lo_done, 8 * q + 2 * r)
                for b, no in enumerate(nos):
                    half = slice(b * CH, (b + 1) * CH)
                    act.copy(wc_raw[half, :], cond_table[half, bass.ds(no, 1), :].rearrange("p a n -> p (a n)")
                             ).then_inc(wc_raw_done, 1)
                act.wait_ge(wc_raw_done, 8 * q + 2 * r + 2)
                for b in range(2):
                    half = slice(b * CH, (b + 1) * CH)
                    act.copy(wc[half, 0, half], wc_raw[half, :]).then_inc(wc_hi_done, 1)

            def yT_high(q, r):
                if r >= 2 or not isinstance(q, int):
                    act.wait_ge(main_done, 12 * q + 3 * (r - 2) + 3)
                for b in range(2):
                    act.wait_ge(y_summed, 16 * q + 4 * r + 2 * b + 2)
                    act.copy(yT[:, r % 2, 0, b * 512:(b + 1) * 512], y32[:, b * 512:(b + 1) * 512]).then_inc(yT_hi_done, 1)

            def adapter_high(q, r):
                if r >= 1 or not isinstance(q, int):
                    act.wait_ge(low_done, 8 * q + 2 * r)
                for b in range(2):
                    e = act.value_load(ids[0:1, bass.ds(SAMPLES + 8 * q + 2 * r + b, 1)],
                                       min_val=0, max_val=EXPERTS - 1)
                    act.copy(adapter[:, :, b, 0, :],
                             folded[:, bass.ds(e, 1), :, :].rearrange("p a k n -> p (a k) n")
                             ).then_inc(adapter_hi_done, 1)

            def x1T_high(q, r):
                if r >= 1 or not isinstance(q, int):
                    act.wait_ge(low_done, 8 * q + 2 * r)
                for b in range(2):
                    act.wait_ge(x1T_done, 8 * q + 2 * r + b + 1)
                    act.copy(x1T_part(b, 0), turned(b)).then_inc(x1T_hi_done, 1)

            def top_exps(q, r):
                act.wait_ge(route_step, ROUTE_STEPS * (4 * q + r) + 3)
                act.activation(top_exp[:, :], top8[:, 0:2], ACT.Exp, bias=neg_max0[:, 0:1],
                               accum_out=top_sum[:, :]).then_inc(top_exp_done, 1)

            def score_exps(q, r):
                act.wait_ge(score_step, SCORE_STEPS * (4 * q + r) + 3)
                act.activation(exp1[:, :], logits1[:, :], ACT.Exp, bias=neg_max1[:, 0:1],
                               accum_out=sum1[:, :]).then_inc(exp1_done, 1)

            def hwT_high(q, r):
                act.wait_ge(hwT_done, 4 * q + r + 1)
                if r >= 1 or not isinstance(q, int):
                    act.wait_ge(main_done, 12 * q + 3 * r)
                act.copy(hwT_hi[:, :], out_ps[0][:, 0:P]).then_inc(hwT_hi_done, 1)

            def lwT_high(q, r):
                act.wait_ge(lwT_done, 4 * q + r + 1)
                if r >= 1 or not isinstance(q, int):
                    act.wait_ge(out_done, 8 * q + 2 * r)
                act.copy(lwT_hi[:, :], low_ps[:, 0:P]).then_inc(lwT_hi_done, 1)

            def iteration(q, r, l0=True, l1=True, ahead=True, ahead2=True):
                if ahead2:
                    nos = cond_nos(q, r + 2)
                if ahead:
                    yT_high(q, r + 1)
                if l1:
                    x1T_high(q, r - 1)
                if l0:
                    top_exps(q, r)
                if ahead2:
                    x_high(q, r + 2)
                    cond_high(q, r + 2, nos)
                if l0:
                    hwT_high(q, r)
                if l1:
                    score_exps(q, r - 1)
                if l1:
                    lwT_high(q, r - 1)
                if l0:
                    adapter_high(q, r)

            act.wait_ge(const_set, 6)
            x_high(0, 0)
            cond_high(0, 0, cond_nos(0, 0))
            yT_high(0, 0)
            x_high(0, 1)
            cond_high(0, 1, cond_nos(0, 1))
            iteration(0, 0, l1=False)
            iteration(0, 1)
            with act.Fori(0, (TILES - 4) // 4) as q:
                for r in range(2, 6):
                    iteration(q, r)
            iteration(0, TILES - 2, ahead2=False)
            iteration(0, TILES - 1, ahead=False, ahead2=False)
            iteration(0, TILES, l0=False, ahead=False, ahead2=False)

        @block.vector
        def _(dve):
            for e in range(EXPERTS):
                last = dve.memset(expert_no[:, e:e + 1], float(e))
            last.then_inc(expert_no_set, 1)
            dve.memset(top_sum[:, :], 0.0).then_inc(unit_lo, RING)
            dve.memset(top_inv[:, :], 0.0).then_inc(unit_done, RING)
            dve.memset(inv1[:, :], 0.0).then_inc(unit_copied, BANKS)

            def plan_after(instruction, step):
                instruction.then_inc(plan_step, 1)
                dve.wait_ge(plan_step, step)

            over_e = [1, EXPERTS, EXPERTS]
            e_rows = expert_no[0:1, :].unsqueeze(2).to_broadcast(over_e)
            e_cols = expert_no[0:1, :].unsqueeze(1).to_broadcast(over_e)
            dve.wait_ge(expert_no_set, 1)
            dve.wait_ge(ids_landed, 16)
            plan_after(dve.tensor_copy(ids_f[:, :], ids[:, SAMPLES:]), 1)
            plan_after(dve.tensor_tensor(asks[:, :, :], ids_f[:, :].unsqueeze(1).to_broadcast([1, EXPERTS, SAMPLES]),
                                         expert_no[0:1, :].unsqueeze(2).to_broadcast([1, EXPERTS, SAMPLES]),
                                         ALU.is_equal), 2)
            plan_after(dve.reduce_max(used[:, :], asks[:, :, :], AX.X), 3)
            plan_after(dve.tensor_tensor(lower[:, :, :], e_cols, e_rows, ALU.is_lt), 4)
            plan_after(dve.tensor_tensor(lower[:, :, :], lower[:, :, :],
                                         used[:, :].unsqueeze(1).to_broadcast(over_e), ALU.mult), 5)
            plan_after(dve.reduce_sum(used_before[:, :], lower[:, :, :], AX.X), 6)
            plan_after(dve.tensor_tensor(used_no[:, :], used[:, :], expert_no[0:1, :], ALU.mult), 7)
            plan_after(dve.tensor_tensor(pairs[:, :, :], used_before[:, :].unsqueeze(1).to_broadcast(over_e),
                                         e_rows, ALU.is_equal), 8)
            plan_after(dve.tensor_tensor(pairs[:, :, :], pairs[:, :, :],
                                         used_no[:, :].unsqueeze(1).to_broadcast(over_e), ALU.mult), 9)
            dve.reduce_sum(plan_f[:, 0:EXPERTS], pairs[:, :, :], AX.X)
            plan_after(dve.reduce_sum(plan_f[:, EXPERTS:], used[:, :], AX.X), 10)
            plan_after(dve.tensor_copy(plan[:, :], plan_f[:, :]), 11)

            dve.wait_ge(ag1_hi_done, 1)
            dve.tensor_tensor(ag1_cut[:, :, 1, :], ag1_raw, ag1_cut[:, :, 0, :], ALU.subtract
                              ).then_inc(ag1_lo_done, 1)

            def sum_unit(n, c, e):
                dve.wait_ge(unit_done, KC * n + c + 1 + RING)
                dve.reduce_sum(folded[:, bass.ds(e, 1), c, :].rearrange("p a n -> p (a n)"),
                               main_ps[c % BANKS][:, 0:2 * HG].rearrange("p (h n) -> p n h", h=2), AX.X
                               ).then_inc(unit_copied, 1)

            in_use = adapters_in_use(dve)
            with dve.Fori(0, in_use) as n:
                e = adapter_at(dve, n)
                for c in range(KC):
                    dve.wait_ge(unit_hi, KC * n + c + 1)
                    hi, lo = unit_cut[c % RING]
                    dve.tensor_tensor(lo, ring[:, c % RING, :], hi, ALU.subtract).then_inc(unit_lo, 1)
                    if c >= 1:
                        sum_unit(n, c - 1, e)
                sum_unit(n, KC - 1, e)
            dve.wait_ge(side_lo, len(sides))
            dve.wait_ge(small_landed, 64)
            dve.wait_ge(const_set, 6)

            def cond_low(q, r):
                for b in range(2):
                    dve.wait_ge(wc_hi_done, 8 * q + 2 * r + b + 1)
                    half = slice(b * CH, (b + 1) * CH)
                    dve.tensor_tensor(wc[half, 1, half], wc_raw[half, :], wc[half, 0, half], ALU.subtract
                                      ).then_inc(wc_lo_done, 1)

            def sum_y(q, r, batch):
                if r >= 1 or not isinstance(q, int):
                    dve.wait_ge(yT_lo_done, 8 * q + 2 * (r - 1) + batch + 1)
                for n in range(2):
                    pair = 2 * batch + n
                    bank = turn_ps[n][:, :].rearrange("p (c h n) -> p c n h", c=2, h=2)
                    dve.wait_ge(yT_done, 16 * q + 4 * r + pair + 1)
                    dve.reduce_sum(y32[:, pair * 2 * P:(pair + 1) * 2 * P].rearrange("p (c n) -> p c n", c=2),
                                   bank, AX.X).then_inc(y_summed, 1)

            def x1T_low(q, r):
                for b in range(2):
                    dve.wait_ge(x1T_hi_done, 8 * q + 2 * r + b + 1)
                    dve.tensor_tensor(x1T_part(b, 1), turned(b), x1T_part(b, 0), ALU.subtract
                                      ).then_inc(x1T_lo_done, 1)

            def final(q, r):
                for b in range(2):
                    row = ring[:, r % RING, b * 512:(b + 1) * 512]
                    dve.wait_ge(out_done, 8 * q + 2 * r + b + 1)
                    dve.tensor_tensor(row, row, out_ps[b][:, :], ALU.add).then_inc(final_done, 1)

            def copy_hg(q, r):
                dve.wait_ge(hg_done, 4 * q + r + 1)
                dve.tensor_copy(hg[:, :], main_ps[0][:, 0:HG]).then_inc(hg_copied, 1)

            def routing(q, r):
                def step(instruction, n):
                    instruction.then_inc(route_step, 1)

                def after(n):
                    dve.wait_ge(route_step, ROUTE_STEPS * (4 * q + r) + n)
                dve.wait_ge(hg_copied, 4 * q + r + 1)
                logits = hg[:, HR:HG]
                step(dve.reduce_max(max0[:, :], logits, AX.X), 1)
                step(dve.max(top8[:, :], logits), 2)
                after(2)
                step(dve.tensor_scalar(neg_max0[:, :], max0[:, :], -1.0, None, ALU.mult), 3)
                step(dve.max_index(top_at[:, :], top8[:, :], logits), 4)
                after(4)
                step(dve.tensor_copy(top_no[:, :], top_at[:, 0:2]), 5)
                dve.wait_ge(top_exp_done, 4 * q + r + 1)
                step(dve.reciprocal(top_inv[:, :], top_sum[:, :]), 6)
                after(6)
                step(dve.tensor_scalar(top_w[:, :], top_exp[:, :], top_inv[:, 0:1], None, ALU.mult), 7)
                after(7)
                step(dve.tensor_scalar(route_a[:, :], expert_no[:, :], top_no[:, 0:1], top_w[:, 0:1],
                                       ALU.is_equal, ALU.mult), 8)
                step(dve.tensor_scalar(route_b[:, :], expert_no[:, :], top_no[:, 1:2], top_w[:, 1:2],
                                       ALU.is_equal, ALU.mult), 9)
                after(9)
                step(dve.tensor_tensor(route[:, :], route_a[:, :], route_b[:, :], ALU.add), 10)
                after(10)
                if r >= 1 or not isinstance(q, int):
                    dve.wait_ge(hwT_done, 4 * q + r)
                step(dve.tensor_tensor(hw[:, :].rearrange("p (e k) -> p e k", k=RANK),
                                       hg[:, 0:HR].rearrange("p (e k) -> p e k", k=RANK),
                                       route[:, :].unsqueeze(2).to_broadcast([P, EXPERTS, RANK]),
                                       ALU.mult), 11)

            def sum_low(q, r, b):
                bank = (low_ps, turn_ps[0])[b]
                mine = slice(b * CH, (b + 1) * CH)
                dve.wait_ge(low_done, 8 * q + 2 * r + b + 1)
                for part, name in enumerate((low_hi, low_lo)):
                    rows = slice(part * CH, (part + 1) * CH)
                    dve.reduce_sum(name[mine, :], bank[rows, 0:2 * HG].rearrange("p (h n) -> p n h", h=2), AX.X
                                   ).then_inc(halves_summed, 1)
                dve.wait_ge(halves_summed, 16 * q + 4 * r + 2 * b + 2)
                dve.tensor_tensor(lg[mine, :], low_hi[mine, :], low_lo[mine, :], ALU.add).then_inc(lg_done, 1)

            def score_after(q, r, n):
                dve.wait_ge(score_step, SCORE_STEPS * (4 * q + r) + n)

            def score_logits(q, r):
                def after(n):
                    score_after(q, r, n)
                dve.wait_ge(lg_done, 8 * q + 2 * r + 2)
                dve.tensor_tensor(logits1[:, :], lg[:, HR:HG], br_rows[:, :], ALU.add).then_inc(score_step, 1)
                after(1)
                dve.reduce_max(max1[:, :], logits1[:, :], AX.X).then_inc(score_step, 1)
                after(2)
                dve.tensor_scalar(neg_max1[:, :], max1[:, :], -1.0, None, ALU.mult).then_inc(score_step, 1)

            def scoring(q, r):
                def after(n):
                    score_after(q, r, n)
                dve.wait_ge(exp1_done, 4 * q + r + 1)
                dve.reciprocal(inv1[:, :], sum1[:, :]).then_inc(score_step, 1)
                after(4)
                dve.tensor_scalar(score[:, :], exp1[:, :], inv1[:, 0:1], L1_SCALE,
                                  ALU.mult, ALU.mult).then_inc(score_step, 1)
                after(5)
                if r >= 1 or not isinstance(q, int):
                    dve.wait_ge(lwT_done, 4 * q + r)
                dve.tensor_tensor(lw[:, :].rearrange("p (e k) -> p e k", k=RANK),
                                  lg[:, 0:HR].rearrange("p (e k) -> p e k", k=RANK),
                                  score[:, :].unsqueeze(2).to_broadcast([P, EXPERTS, RANK]),
                                  ALU.mult).then_inc(score_step, 2)

            def hwT_low(q, r):
                dve.wait_ge(hwT_hi_done, 4 * q + r + 1)
                dve.tensor_tensor(hwT_lo[:, :], out_ps[0][:, 0:P], hwT_hi[:, :], ALU.subtract
                                  ).then_inc(hwT_lo_done, 1)

            def lwT_low(q, r):
                dve.wait_ge(lwT_hi_done, 4 * q + r + 1)
                dve.tensor_tensor(lwT_lo[:, :], low_ps[:, 0:P], lwT_hi[:, :], ALU.subtract
                                  ).then_inc(lwT_lo_done, 1)

            def add_base(q, r, g):
                a, b = GROUPS[g]
                a0 = max(a, HG)
                row = ring[:, r % RING, a0 - HG:b - HG]
                dve.tensor_tensor(row, row, main_ps[g][:, a0 - a:b - a], ALU.add).then_inc(x1_done, 1)

            def iteration(q, r, l0=True, l1=True, l1_out=True, ahead=True, ahead2=True):
                if l1_out:
                    final(q, r - 2)
                if ahead:
                    sum_y(q, r + 1, 0)
                if l0:
                    copy_hg(q, r)
                if ahead:
                    sum_y(q, r + 1, 1)
                if l1:
                    x1T_low(q, r - 1)
                if l0:
                    routing(q, r)
                if l1:
                    sum_low(q, r - 1, 0)
                    sum_low(q, r - 1, 1)
                if l1:
                    score_logits(q, r - 1)
                if l0:
                    hwT_low(q, r)
                if l1:
                    scoring(q, r - 1)
                if ahead2:
                    cond_low(q, r + 2)
                if l1:
                    lwT_low(q, r - 1)
                if l0:
                    dve.wait_ge(xb_done, 4 * q + r + 1)
                    for g in range(3):
                        dve.wait_ge(main_done, 12 * q + 3 * r + g + 1)
                        add_base(q, r, g)

            cond_low(0, 0)
            sum_y(0, 0, 0)
            sum_y(0, 0, 1)
            cond_low(0, 1)
            iteration(0, 0, l1=False, l1_out=False)
            iteration(0, 1, l1_out=False)
            with dve.Fori(0, (TILES - 4) // 4) as q:
                for r in range(2, 6):
                    iteration(q, r)
            iteration(0, TILES - 2, ahead2=False)
            iteration(0, TILES - 1, ahead=False, ahead2=False)
            iteration(0, TILES, l0=False, ahead=False, ahead2=False)
            final(0, TILES - 1)

        @block.gpsimd
        def _(pool):
            pool.memset(identity[:, :], 0.0).then_inc(const_set, 1)
            pool.memset(wc[:, :, :].bitcast(F32), 0.0).then_inc(const_set, 2)
            pool.memset(zero_cols[:, :], 0.0).then_inc(const_set, 1)
            pool.wait_ge(const_set, 4)
            pool.affine_select(out=identity[:, :], in_=identity[:, :], compare_op=ALU.not_equal, fill=1.0,
                               base=0, pattern=[[-1, P]], channel_multiplier=1).then_inc(const_set, 2)

            def load_side(n):
                width, src, _, _ = sides[n]
                pool.dma_start(side_raw[n % 2][:, 0:width], src).then_inc(side_landed[n % 2], 16)

            load_side(0)
            load_side(1)
            for n, (width, _, hi, lo) in enumerate(sides):
                raw = side_raw[n % 2][:, 0:width]
                pool.wait_ge(side_landed[n % 2], 16 * (n // 2 + 1))
                pool.tensor_tensor(hi, raw, zero_cols[:, :].to_broadcast([P, width]), ALU.add).then_inc(side_hi, 1)
                pool.wait_ge(side_hi, n + 1)
                pool.tensor_tensor(lo, raw, hi, ALU.subtract).then_inc(side_lo, 1)
                if n + 2 < len(sides):
                    pool.wait_ge(side_lo, n + 1)
                    load_side(n + 2)
            pool.wait_ge(side_lo, len(sides))
            pool.dma_start(bias_rows[:, :], bias.partition_broadcast(P)).then_inc(bias_landed, 16)
            pool.wait_ge(bias_landed, 16)
            pool.wait_ge(small_landed, 64)
            pool.wait_ge(ids_landed, 16)

            def x_low(q, r):
                pool.wait_ge(x_hi_done, 4 * q + r + 1)
                row = ring[:, r % RING, :]
                pool.tensor_tensor(x_lo[:, :], row, x_hi[:, :], ALU.subtract).then_inc(x_lo_done, 1)
                pool.wait_ge(x_lo_done, 4 * q + r + 1)
                pool.tensor_tensor(row, row, bias_rows[:, :], ALU.add).then_inc(xb_done, 1)

            def adapter_low(q, r):
                if r >= 1 or not isinstance(q, int):
                    pool.wait_ge(adapter_lo_done, 8 * q + 2 * r)
                pool.wait_ge(adapter_hi_done, 8 * q + 2 * r + 2)
                pool.tensor_tensor(wait_col[:, :], zero_cols[:, :], zero_cols[:, :], ALU.add)
                for b in range(2):
                    e = pool.value_load(ids[0:1, bass.ds(SAMPLES + 8 * q + 2 * r + b, 1)],
                                        min_val=0, max_val=EXPERTS - 1)
                    pool.tensor_tensor(adapter[:, :, b, 1, :],
                                       folded[:, bass.ds(e, 1), :, :].rearrange("p a k n -> p (a k) n"),
                                       adapter[:, :, b, 0, :], ALU.subtract).then_inc(adapter_lo_done, 1)

            def yT_low(q, r):
                if r >= 2 or not isinstance(q, int):
                    pool.wait_ge(main_done, 12 * q + 3 * (r - 2) + 3)
                for b in range(2):
                    cols = slice(b * 512, (b + 1) * 512)
                    pool.wait_ge(yT_hi_done, 8 * q + 2 * r + b + 1)
                    pool.tensor_tensor(yT[:, r % 2, 1, cols], y32[:, cols], yT[:, r % 2, 0, cols], ALU.subtract
                                       ).then_inc(yT_lo_done, 1)

            def iteration(q, r, ahead=True, ahead2=True):
                if ahead:
                    yT_low(q, r + 1)
                if ahead2:
                    x_low(q, r + 2)
                adapter_low(q, r)

            x_low(0, 0)
            yT_low(0, 0)
            x_low(0, 1)
            iteration(0, 0)
            iteration(0, 1)
            with pool.Fori(0, (TILES - 4) // 4) as q:
                for r in range(2, 6):
                    iteration(q, r)
            iteration(0, TILES - 2, ahead2=False)
            iteration(0, TILES - 1, ahead=False, ahead2=False)


def kernel(**inputs):
    import numpy as np
    import concourse.bacc as bacc
    from concourse.bass_utils import run_bass_kernel_spmd

    def get(name):
        return np.asarray(inputs[name])

    def chunked(a, columns):
        return a.reshape(KC, P, columns).transpose(1, 0, 2).reshape(P, KC * columns)

    w0 = np.concatenate([get("L0_ffn_A").reshape(HR, D), get("L0_ffn_W_gate"), get("L0_ffn_W_base")], axis=0)
    ag1 = np.concatenate([get("L1_ffn_A").reshape(HR, D), get("L1_ffn_Wr")], axis=0)
    w1 = get("L1_cond_weight").reshape(EXPERTS, KC, P, KC, P).transpose(0, 3, 2, 1, 4).reshape(UNITS, P, D)
    arrays = {
        "x": get("x").reshape(TILES, P, D),
        "cond_ids": get("itok_B_0_15").reshape(1, SAMPLES),
        "adapter_ids": get("itok_B_3_7").reshape(1, SAMPLES),
        "w_cond": get("L0_cond_weights").transpose(1, 0, 2),
        "w0": chunked(w0.T, NW),
        "bias": get("L0_ffn_b_base"),
        "b0": get("L0_ffn_B").transpose(0, 2, 1).reshape(HR, D),
        "w1": w1,
        "ag1": chunked(ag1.T, HG),
        "b1": get("L1_ffn_B").transpose(0, 2, 1).reshape(HR, D),
        "br": get("L1_ffn_br"),
    }
    nc = bacc.Bacc("TRN2", target_bir_lowering=False, num_devices=1)
    args = []
    feed = {}
    for name, a in arrays.items():
        a = np.ascontiguousarray(a)
        feed["in_" + name] = a
        args.append(nc.dram_tensor("in_" + name, a.shape, mybir.dt.from_np(a.dtype), kind="ExternalInput").ap())
    out = nc.dram_tensor("out", (TILES, P, D), F32, kind="ExternalOutput").ap()
    build(nc, *args, out)
    result = run_bass_kernel_spmd(nc, [feed], core_ids=[0])
    return result.results[0]["out"].reshape(SAMPLES, CH, D)
```
